# Optimizing a Trainium2 kernel written in Bass

```python
import numpy as np
import jax
import jax.numpy as jnp

def _softmax(x, axis=-1):
    return jax.nn.softmax(x, axis=axis)

def _gelu(x):
    return jax.nn.gelu(x, approximate=True)

def _silu(x):
    return jax.nn.silu(x)

def _sigmoid(x):
    return jax.nn.sigmoid(x)

def _layernorm(x, axis=-1, eps=1e-05):
    m = jnp.mean(x, axis=axis, keepdims=True)
    v = jnp.var(x, axis=axis, keepdims=True)
    return (x - m) / jnp.sqrt(v + eps)

def _scatter_add(tgt, idx, src, axis=0):
    return tgt.at[idx].add(src)

def _segment_sum(src, seg, n):
    return jax.ops.segment_sum(src, seg, n)
kernel_name = 'mk_dlrm_tower_d1_rec_r8_2623c5'

def setup_inputs(seed: int=0):
    np.random.seed(seed)
    _w = jnp.asarray

    def _rec_inputs():
        import jax
        import jax.numpy as jnp
        _tk = jax.random.key(seed)
        dense_ctx = jax.random.normal(jax.random.fold_in(_tk, 190), (512, 16), jnp.float32)
        ids = jnp.stack([jax.random.randint(jax.random.fold_in(_tk, 200 + f), (512,), 0, v, jnp.int32) for f, v in enumerate([125000, 12500, 1000, 1000, 1000, 125000, 1250, 12500, 1250, 12500, 12500, 125000, 1000, 12500, 1250, 12500, 1250, 1000, 1250, 1250, 1250, 1250, 1250, 1250, 1000, 1250, 12500, 1000, 1000, 1000, 1250, 1250, 1000, 1000, 1000, 1000, 1000, 1000, 1250, 1250])], axis=1)
        tbl_0 = 0.05 * jax.random.normal(jax.random.fold_in(_tk, 500 + 0), (125000, 64), jnp.float32)
        tbl_1 = 0.05 * jax.random.normal(jax.random.fold_in(_tk, 500 + 1), (12500, 64), jnp.float32)
        tbl_2 = 0.05 * jax.random.normal(jax.random.fold_in(_tk, 500 + 2), (1000, 64), jnp.float32)
        tbl_3 = 0.05 * jax.random.normal(jax.random.fold_in(_tk, 500 + 3), (1000, 64), jnp.float32)
        tbl_4 = 0.05 * jax.random.normal(jax.random.fold_in(_tk, 500 + 4), (1000, 64), jnp.float32)
        tbl_5 = 0.05 * jax.random.normal(jax.random.fold_in(_tk, 500 + 5), (125000, 64), jnp.float32)
        tbl_6 = 0.05 * jax.random.normal(jax.random.fold_in(_tk, 500 + 6), (1250, 64), jnp.float32)
        tbl_7 = 0.05 * jax.random.normal(jax.random.fold_in(_tk, 500 + 7), (12500, 64), jnp.float32)
        tbl_8 = 0.05 * jax.random.normal(jax.random.fold_in(_tk, 500 + 8), (1250, 64), jnp.float32)
        tbl_9 = 0.05 * jax.random.normal(jax.random.fold_in(_tk, 500 + 9), (12500, 64), jnp.float32)
        tbl_10 = 0.05 * jax.random.normal(jax.random.fold_in(_tk, 500 + 10), (12500, 64), jnp.float32)
        tbl_11 = 0.05 * jax.random.normal(jax.random.fold_in(_tk, 500 + 11), (125000, 64), jnp.float32)
        tbl_12 = 0.05 * jax.random.normal(jax.random.fold_in(_tk, 500 + 12), (1000, 64), jnp.float32)
        tbl_13 = 0.05 * jax.random.normal(jax.random.fold_in(_tk, 500 + 13), (12500, 64), jnp.float32)
        tbl_14 = 0.05 * jax.random.normal(jax.random.fold_in(_tk, 500 + 14), (1250, 64), jnp.float32)
        tbl_15 = 0.05 * jax.random.normal(jax.random.fold_in(_tk, 500 + 15), (12500, 64), jnp.float32)
        tbl_16 = 0.05 * jax.random.normal(jax.random.fold_in(_tk, 500 + 16), (1250, 64), jnp.float32)
        tbl_17 = 0.05 * jax.random.normal(jax.random.fold_in(_tk, 500 + 17), (1000, 64), jnp.float32)
        tbl_18 = 0.05 * jax.random.normal(jax.random.fold_in(_tk, 500 + 18), (1250, 64), jnp.float32)
        tbl_19 = 0.05 * jax.random.normal(jax.random.fold_in(_tk, 500 + 19), (1250, 64), jnp.float32)
        tbl_20 = 0.05 * jax.random.normal(jax.random.fold_in(_tk, 500 + 20), (1250, 64), jnp.float32)
        tbl_21 = 0.05 * jax.random.normal(jax.random.fold_in(_tk, 500 + 21), (1250, 64), jnp.float32)
        tbl_22 = 0.05 * jax.random.normal(jax.random.fold_in(_tk, 500 + 22), (1250, 64), jnp.float32)
        tbl_23 = 0.05 * jax.random.normal(jax.random.fold_in(_tk, 500 + 23), (1250, 64), jnp.float32)
        tbl_24 = 0.05 * jax.random.normal(jax.random.fold_in(_tk, 500 + 24), (1000, 64), jnp.float32)
        tbl_25 = 0.05 * jax.random.normal(jax.random.fold_in(_tk, 500 + 25), (1250, 64), jnp.float32)
        tbl_26 = 0.05 * jax.random.normal(jax.random.fold_in(_tk, 500 + 26), (12500, 64), jnp.float32)
        tbl_27 = 0.05 * jax.random.normal(jax.random.fold_in(_tk, 500 + 27), (1000, 64), jnp.float32)
        tbl_28 = 0.05 * jax.random.normal(jax.random.fold_in(_tk, 500 + 28), (1000, 64), jnp.float32)
        tbl_29 = 0.05 * jax.random.normal(jax.random.fold_in(_tk, 500 + 29), (1000, 64), jnp.float32)
        tbl_30 = 0.05 * jax.random.normal(jax.random.fold_in(_tk, 500 + 30), (1250, 64), jnp.float32)
        tbl_31 = 0.05 * jax.random.normal(jax.random.fold_in(_tk, 500 + 31), (1250, 64), jnp.float32)
        tbl_32 = 0.05 * jax.random.normal(jax.random.fold_in(_tk, 500 + 32), (1000, 64), jnp.float32)
        tbl_33 = 0.05 * jax.random.normal(jax.random.fold_in(_tk, 500 + 33), (1000, 64), jnp.float32)
        tbl_34 = 0.05 * jax.random.normal(jax.random.fold_in(_tk, 500 + 34), (1000, 64), jnp.float32)
        tbl_35 = 0.05 * jax.random.normal(jax.random.fold_in(_tk, 500 + 35), (1000, 64), jnp.float32)
        tbl_36 = 0.05 * jax.random.normal(jax.random.fold_in(_tk, 500 + 36), (1000, 64), jnp.float32)
        tbl_37 = 0.05 * jax.random.normal(jax.random.fold_in(_tk, 500 + 37), (1000, 64), jnp.float32)
        tbl_38 = 0.05 * jax.random.normal(jax.random.fold_in(_tk, 500 + 38), (1250, 64), jnp.float32)
        tbl_39 = 0.05 * jax.random.normal(jax.random.fold_in(_tk, 500 + 39), (1250, 64), jnp.float32)
        _rk = jax.random.fold_in(_tk, 7)
        W_top1 = 0.0354441 * jax.random.normal(jax.random.fold_in(_tk, 801), (796, 512), jnp.float32)
        W_top2 = 0.0441942 * jax.random.normal(jax.random.fold_in(_tk, 802), (512, 256), jnp.float32)
        W_top3 = 0.0625 * jax.random.normal(jax.random.fold_in(_tk, 803), (256, 1), jnp.float32)
        b_top1 = jnp.zeros((512,), jnp.float32)
        b_top2 = jnp.zeros((256,), jnp.float32)
        return (dense_ctx, ids, tbl_0, tbl_1, tbl_2, tbl_3, tbl_4, tbl_5, tbl_6, tbl_7, tbl_8, tbl_9, tbl_10, tbl_11, tbl_12, tbl_13, tbl_14, tbl_15, tbl_16, tbl_17, tbl_18, tbl_19, tbl_20, tbl_21, tbl_22, tbl_23, tbl_24, tbl_25, tbl_26, tbl_27, tbl_28, tbl_29, tbl_30, tbl_31, tbl_32, tbl_33, tbl_34, tbl_35, tbl_36, tbl_37, tbl_38, tbl_39, W_top1, b_top1, W_top2, b_top2, W_top3)
    dense_ctx, ids, tbl_0, tbl_1, tbl_2, tbl_3, tbl_4, tbl_5, tbl_6, tbl_7, tbl_8, tbl_9, tbl_10, tbl_11, tbl_12, tbl_13, tbl_14, tbl_15, tbl_16, tbl_17, tbl_18, tbl_19, tbl_20, tbl_21, tbl_22, tbl_23, tbl_24, tbl_25, tbl_26, tbl_27, tbl_28, tbl_29, tbl_30, tbl_31, tbl_32, tbl_33, tbl_34, tbl_35, tbl_36, tbl_37, tbl_38, tbl_39, W_top1, b_top1, W_top2, b_top2, W_top3 = _rec_inputs()

    def _L0_rec_setup():
        import jax, jax.numpy as jnp
        import numpy as np

        def _pair_indices(num_fields):
            i_idx, j_idx = np.triu_indices(num_fields, k=1)
            return (jnp.asarray(i_idx), jnp.asarray(j_idx))
        key = jax.random.key(seed)
        k1, k2 = jax.random.split(key)
        B, F, D = (256, 40, 64)
        P = F * (F - 1) // 2
        x = jax.random.normal(k1, (B, F, D), dtype=jnp.float32)
        W = jax.random.normal(k2, (P, D, D), dtype=jnp.float32) * (1.0 / np.sqrt(D))
        return {'x': x, 'W': W}
    _L0_rec_all = _L0_rec_setup()
    _L0_rec_in = {k: v for k, v in _L0_rec_all.items() if k in ('W',)}
    del _L0_rec_all
    return {'dense_ctx': dense_ctx, 'ids': ids, 'tbl_0': tbl_0, 'tbl_1': tbl_1, 'tbl_2': tbl_2, 'tbl_3': tbl_3, 'tbl_4': tbl_4, 'tbl_5': tbl_5, 'tbl_6': tbl_6, 'tbl_7': tbl_7, 'tbl_8': tbl_8, 'tbl_9': tbl_9, 'tbl_10': tbl_10, 'tbl_11': tbl_11, 'tbl_12': tbl_12, 'tbl_13': tbl_13, 'tbl_14': tbl_14, 'tbl_15': tbl_15, 'tbl_16': tbl_16, 'tbl_17': tbl_17, 'tbl_18': tbl_18, 'tbl_19': tbl_19, 'tbl_20': tbl_20, 'tbl_21': tbl_21, 'tbl_22': tbl_22, 'tbl_23': tbl_23, 'tbl_24': tbl_24, 'tbl_25': tbl_25, 'tbl_26': tbl_26, 'tbl_27': tbl_27, 'tbl_28': tbl_28, 'tbl_29': tbl_29, 'tbl_30': tbl_30, 'tbl_31': tbl_31, 'tbl_32': tbl_32, 'tbl_33': tbl_33, 'tbl_34': tbl_34, 'tbl_35': tbl_35, 'tbl_36': tbl_36, 'tbl_37': tbl_37, 'tbl_38': tbl_38, 'tbl_39': tbl_39, 'W_top1': W_top1, 'b_top1': b_top1, 'W_top2': W_top2, 'b_top2': b_top2, 'W_top3': W_top3, 'L0_rec_W': _L0_rec_in['W']}

def reference(dense_ctx, ids, tbl_0, tbl_1, tbl_2, tbl_3, tbl_4, tbl_5, tbl_6, tbl_7, tbl_8, tbl_9, tbl_10, tbl_11, tbl_12, tbl_13, tbl_14, tbl_15, tbl_16, tbl_17, tbl_18, tbl_19, tbl_20, tbl_21, tbl_22, tbl_23, tbl_24, tbl_25, tbl_26, tbl_27, tbl_28, tbl_29, tbl_30, tbl_31, tbl_32, tbl_33, tbl_34, tbl_35, tbl_36, tbl_37, tbl_38, tbl_39, W_top1, b_top1, W_top2, b_top2, W_top3, L0_rec_W):
    import jax
    import jax.numpy as jnp

    def _L0_rec_ref(x, W):
        import jax, jax.numpy as jnp
        import numpy as np

        def _pair_indices(num_fields):
            i_idx, j_idx = np.triu_indices(num_fields, k=1)
            return (jnp.asarray(i_idx), jnp.asarray(j_idx))
        B, F, D = x.shape
        i_idx, j_idx = _pair_indices(F)
        vi = x[:, i_idx, :]
        vj = x[:, j_idx, :]
        viW = jnp.einsum('bpd,pde->bpe', vi, W)
        out = jnp.einsum('bpe,bpe->bp', viW, vj)
        return out
    e = jnp.stack([tbl_0[ids[:, 0]], tbl_1[ids[:, 1]], tbl_2[ids[:, 2]], tbl_3[ids[:, 3]], tbl_4[ids[:, 4]], tbl_5[ids[:, 5]], tbl_6[ids[:, 6]], tbl_7[ids[:, 7]], tbl_8[ids[:, 8]], tbl_9[ids[:, 9]], tbl_10[ids[:, 10]], tbl_11[ids[:, 11]], tbl_12[ids[:, 12]], tbl_13[ids[:, 13]], tbl_14[ids[:, 14]], tbl_15[ids[:, 15]], tbl_16[ids[:, 16]], tbl_17[ids[:, 17]], tbl_18[ids[:, 18]], tbl_19[ids[:, 19]], tbl_20[ids[:, 20]], tbl_21[ids[:, 21]], tbl_22[ids[:, 22]], tbl_23[ids[:, 23]], tbl_24[ids[:, 24]], tbl_25[ids[:, 25]], tbl_26[ids[:, 26]], tbl_27[ids[:, 27]], tbl_28[ids[:, 28]], tbl_29[ids[:, 29]], tbl_30[ids[:, 30]], tbl_31[ids[:, 31]], tbl_32[ids[:, 32]], tbl_33[ids[:, 33]], tbl_34[ids[:, 34]], tbl_35[ids[:, 35]], tbl_36[ids[:, 36]], tbl_37[ids[:, 37]], tbl_38[ids[:, 38]], tbl_39[ids[:, 39]]], axis=1)
    z = _L0_rec_ref(e, L0_rec_W)
    z = z.reshape(z.shape[0], -1)
    h = jnp.concatenate([z, dense_ctx], axis=1)
    h = jnp.maximum(h @ W_top1 + b_top1, 0.0)
    h = jnp.maximum(h @ W_top2 + b_top2, 0.0)
    y = h @ W_top3
    return y

_drawn_inputs = setup_inputs


def setup_inputs(seed=0):
    import zlib

    import numpy as np

    out = dict(_drawn_inputs(seed))
    spreads = {'b_top1': (0.0, 0.1), 'b_top2': (0.0, 0.1)}
    factors = {}
    for name, (base, spread) in spreads.items():
        noise = np.random.default_rng([zlib.crc32(name.encode()), seed]).standard_normal(out[name].shape)
        drawn = base * np.exp(spread * noise) if base else spread * noise
        out[name] = jnp.asarray(drawn.astype(out[name].dtype))
    for name, factor in factors.items():
        out[name] = (out[name] * factor).astype(out[name].dtype)
    return out
```

```python
from contextlib import ExitStack

import concourse.bass as bass
from concourse import mybir

F32 = mybir.dt.float32
F32R = mybir.dt.float32r
I32 = mybir.dt.int32
ALU = mybir.AluOpType
ACT = mybir.ActivationFunctionType

ROWS = 128
BANK = 512
FIELDS = 40
DIM = 64
BATCH = 512
DENSE = 16
BATCH_TILES = BATCH // ROWS
FIELD_PAIRS = FIELDS // 2
PAIRS = FIELDS * (FIELDS - 1) // 2

GROUP_SIZES = [2] * 6 + [4] * 7
ROUND = 4
CALM_FROM = 12
QUAD = 32

GATHER_SLOTS = 7
RAW_SLOTS = 6
SPLIT_SLOTS = 4
Y_SLOTS = 3
P_SLOTS = 6


def pair_index(i, j):
    return i * FIELDS - i * (i + 1) // 2 + (j - i - 1)


class Plan:

    def __init__(self):
        self.tiles = []
        self.group_start = []
        a = 0
        for size in GROUP_SIZES:
            self.group_start.append(len(self.tiles) // ROUND)
            for i in range(a + size - 1):
                first = max(a, i + 1) // 2 * 2
                self.tiles += [(i, j) for j in range(first, a + size, 2)]
            a += size
        assert a == FIELDS and len(self.tiles) % ROUND == 0
        self.rounds = len(self.tiles) // ROUND
        self.halves = 2 * self.rounds
        self.group_start.append(self.rounds)

        self.rows = []
        block, fill, quad = 0, [0, 0, 0, QUAD], 0
        self.blocks = [[None] * ROWS]
        for q in range(DENSE):
            self.blocks[0][3 * QUAD + q] = PAIRS + q
        for t, (i, j) in enumerate(self.tiles):
            n = 1 if i == j else 2
            free = [(quad + s) % 4 for s in range(4) if fill[(quad + s) % 4] + n <= QUAD]
            if t % 2 == 0 and sum((QUAD - f) // 2 for f in fill) < 2:
                block, fill = block + 1, [0] * 4
                self.blocks.append([None] * ROWS)
                free = [quad]
            quad = free[0]
            row = fill[quad]
            self.rows.append((block, quad, row))
            for s in range(n):
                at = j + 1 if n == 1 else j + s
                self.blocks[block][quad * QUAD + row + s] = pair_index(i, at)
            fill[quad] += n
            quad = (quad + 1) % 4
        assert all(fill), "every quadrant of the last block must be written"
        self.block_last_half = [
            max(t for t in range(len(self.tiles)) if self.rows[t][0] == b) // 2 for b in range(len(self.blocks))
        ]

        self.split_round = []
        k = 0
        for g, size in enumerate(GROUP_SIZES):
            before = self.group_start[g] - (self.group_start[g - 1] if g else 0)
            m = size // 2
            for s in range(m):
                lead = 1 + (m - 1 - s) * min(2, before // m)
                self.split_round.append(max(0, self.group_start[g] - lead))
                k += 1

        self.gather_round = []
        for f in range(FIELDS):
            k = f // 2
            free = self.split_round[k - GATHER_SLOTS] if k >= GATHER_SLOTS else 0
            calm = (k // 2) ** 2 - 10 + 2 * (f % 4) if k >= CALM_FROM else 0
            at = max(free, calm, self.gather_round[-1] if f else 0)
            assert at <= self.split_round[k]
            self.gather_round.append(at)

    def weight_runs(self, r):
        runs = []
        for s, (i, j) in enumerate(self.tiles[ROUND * r:ROUND * r + ROUND]):
            for e in range(2):
                p = max(0, pair_index(i, j + 1) - 1 + e)
                slot = 2 * s + e
                if runs and runs[-1][0] + runs[-1][1] == p:
                    runs[-1][1] += 1
                else:
                    runs.append([p, 1, slot])
        return runs

    def ops_of_half(self, h):
        (i0, j0), (i1, j1) = self.tiles[2 * h:2 * h + 2]
        return [(0, 2)] if j1 == j0 + 2 else [(0, 1), (1, 1)]

    def splits_on_pool(self, r):
        return r >= 22 and (r >= 50 or r % 3 > 0)


def dlrm_tower(nc, dense_ctx, ids, tables, W_top1, b_top1, W_top2, b_top2, W_top3, W, identity, selectors,
               w1_rows, out):
    plan = Plan()
    H1 = W_top1.shape[1]
    H2 = W_top2.shape[1]
    M1, M2 = H1 // ROWS, H2 // ROWS
    NBLK = len(plan.blocks)

    with ExitStack() as ctx:
        def sb(name, shape, dt=F32):
            return ctx.enter_context(nc.sbuf_tensor(name, shape, dt))

        def psum(name, shape):
            return ctx.enter_context(nc.psum_tensor(name, shape, F32))

        def sem(name):
            return ctx.enter_context(nc.semaphore(name))

        ids_sb = sb("ids_sb", [ROWS, BATCH_TILES, FIELDS], I32)
        w1_rows_sb = sb("w1_rows_sb", [ROWS, NBLK], I32)
        ident = sb("ident", [ROWS, ROWS])
        select = sb("select", [ROWS, 2, 2 * QUAD])
        dense = sb("dense", [ROWS, BATCH_TILES, QUAD])
        x_full = sb("x_full", [ROWS, FIELD_PAIRS, BATCH])
        x_split = sb("x_split", [ROWS, FIELDS, BATCH], F32R)
        w_raw = sb("w_raw", [ROWS, RAW_SLOTS, 2 * ROUND, DIM])
        w_hi = sb("w_hi", [ROWS, SPLIT_SLOTS, ROUND * ROWS], F32R)
        w_lo = sb("w_lo", [ROWS, SPLIT_SLOTS, ROUND * ROWS], F32R)
        prod = sb("prod", [ROWS, P_SLOTS, 2, BATCH])
        zT = sb("zT", [ROWS, NBLK, BATCH])
        w1 = sb("w1", [ROWS, NBLK, H1])
        gathered = w1[:, :, :].rearrange("p s (c n) -> p s c n", c=BATCH_TILES)
        assert GATHER_SLOTS <= NBLK and H1 == BATCH_TILES * 2 * DIM
        w2 = sb("w2", [ROWS, M1, H2])
        w3 = sb("w3", [ROWS, M2])
        b1 = sb("b1", [ROWS, M1])
        b2 = sb("b2", [ROWS, M2])
        h1 = x_full[:, 0:M1, :]
        h2 = x_full[:, M1:M1 + M2, :]
        y_row = x_full[0:1, M1 + M2, :]

        y_ps = psum("y_ps", [ROWS, Y_SLOTS, 2, BANK])
        z_ps = psum("z_ps", [ROWS, BANK])
        t_ps = psum("t_ps", [ROWS, BANK])
        h1_ps = [t_ps[:, :], y_ps[:, 0, 0, :], y_ps[:, 0, 1, :], y_ps[:, 1, 0, :]]
        h2_ps = [y_ps[:, 1, 1, :], y_ps[:, 2, 0, :]]
        out_ps = y_ps[0:1, 2, 1, :]
        assert M1 == len(h1_ps) and M2 == len(h2_ps)

        ids_loaded = sem("ids_loaded")
        tables_loaded = sem("tables_loaded")
        head_loaded = sem("head_loaded")
        dense_zeroed = sem("dense_zeroed")
        dense_loaded = sem("dense_loaded")
        w1_rows_loaded = sem("w1_rows_loaded")
        w1_loaded = sem("w1_loaded")
        fields_gathered = [sem(f"fields_gathered{s}") for s in range(GATHER_SLOTS)]
        fields_transposed = sem("fields_transposed")
        x_copied = sem("x_copied")
        x_ready = sem("x_ready")
        raw_loaded = [sem(f"raw_loaded{s}") for s in range(RAW_SLOTS)]
        hi_ready = sem("hi_ready")
        lo_ready_dve = sem("lo_ready_dve")
        lo_ready_pool = sem("lo_ready_pool")
        y_ready = sem("y_ready")
        prod_ready = sem("prod_ready")
        prod_used = sem("prod_used")
        z_saved = sem("z_saved")
        h1_summed = sem("h1_summed")
        h1_ready = sem("h1_ready")
        h2_summed = sem("h2_summed")
        h2_ready = sem("h2_ready")
        out_summed = sem("out_summed")
        out_ready = sem("out_ready")
        out_stored = sem("out_stored")

        raw_count, issued = [], [0] * RAW_SLOTS
        runs = [plan.weight_runs(r) for r in range(plan.rounds)]
        for r in range(plan.rounds):
            issued[r % RAW_SLOTS] += 16 * 2 * len(runs[r])
            raw_count.append(issued[r % RAW_SLOTS])
        pool_rounds = [plan.splits_on_pool(r) for r in range(plan.rounds)]

        def wait_lo(engine, r):
            if pool_rounds[r]:
                engine.wait_ge(lo_ready_pool, sum(pool_rounds[:r + 1]))
            else:
                engine.wait_ge(lo_ready_dve, r + 1 - sum(pool_rounds[:r + 1]))

        def wait_lo_all(engine, r):
            on_pool = sum(pool_rounds[:r + 1])
            if on_pool:
                engine.wait_ge(lo_ready_pool, on_pool)
            if r + 1 - on_pool:
                engine.wait_ge(lo_ready_dve, r + 1 - on_pool)

        WEIGHT_LEAD = SPLIT_SLOTS - 1

        def weights_to_split(r):
            if r == 0:
                return range(min(WEIGHT_LEAD + 1, plan.rounds))
            return [r + WEIGHT_LEAD] if r + WEIGHT_LEAD < plan.rounds else []

        def fields_to_split(r):
            return [k for k in range(FIELD_PAIRS) if plan.split_round[k] == r]

        def split_lo(engine, c):
            slot = c % SPLIT_SLOTS
            return engine.tensor_tensor(
                w_lo[:, slot, :], w_raw[:, c % RAW_SLOTS, :, :].rearrange("p n e -> p (n e)"),
                w_hi[:, slot, :].bitcast(F32), ALU.subtract)

        block = ctx.enter_context(nc.Block())

        @block.sync
        def _(sp):
            sp.dma_start(ids_sb[:, :, :], ids.rearrange("(c p) f -> p c f", p=ROWS)).then_inc(ids_loaded, 16)
            for r in range(plan.rounds):
                slot = r % RAW_SLOTS
                if r >= RAW_SLOTS:
                    wait_lo_all(sp, r - RAW_SLOTS)
                for p, n, at in runs[r]:
                    for half in range(2):
                        sp.dma_start(w_raw[half * DIM:half * DIM + DIM, slot, at:at + n, :],
                                     W[p:p + n, :, :].rearrange("p d e -> d p e")).then_inc(raw_loaded[slot], 16)
            sp.wait_ge(out_ready, 1)
            sp.dma_start(out.rearrange("b o -> o b"), y_row).then_inc(out_stored, 16)
            sp.wait_ge(out_stored, 16)

        @block.gpsimd
        def _(pool):
            def gather(field):
                k, f = field // 2, field % 2
                slot = k % GATHER_SLOTS
                if f == 0 and k >= GATHER_SLOTS:
                    pool.wait_ge(fields_transposed, k - GATHER_SLOTS + 1)
                for c in range(BATCH_TILES):
                    nc.gpsimd.indirect_dma_start(
                        gathered[:, slot, c, f * DIM:f * DIM + DIM], None, tables[field][:, :],
                        bass.IndirectOffsetOnAxis(ap=ids_sb[:, c, field:field + 1], axis=0),
                    ).then_inc(fields_gathered[slot], 16)

            nc.gpsimd.memset(dense[:, :, :], 0.0).then_inc(dense_zeroed, 1)
            pool.wait_ge(ids_loaded, 16)
            for r in range(plan.rounds):
                for field in range(FIELDS):
                    if plan.gather_round[field] == r:
                        gather(field)
                for c in weights_to_split(r):
                    if pool_rounds[c]:
                        pool.wait_ge(hi_ready, c + 1)
                        split_lo(nc.gpsimd, c).then_inc(lo_ready_pool, 1)
                if r == plan.group_start[-2] + 2:
                    pool.wait_ge(w1_rows_loaded, 16)
                    pool.wait_ge(fields_transposed, FIELD_PAIRS)
                    for b in range(NBLK):
                        nc.gpsimd.indirect_dma_start(
                            w1[:, b, :], None, W_top1[:, :],
                            bass.IndirectOffsetOnAxis(ap=w1_rows_sb[:, b:b + 1], axis=0),
                        ).then_inc(w1_loaded, 16)

        @block.scalar
        def _(act):
            act.dma_start(ident[:, :], identity).then_inc(tables_loaded, 16)
            act.dma_start(select[:, :, :], selectors).then_inc(tables_loaded, 16)
            act.wait_ge(dense_zeroed, 1)
            act.dma_start(dense[:, :, 0:DENSE], dense_ctx.rearrange("(c p) q -> p c q", p=ROWS)).then_inc(
                dense_loaded, 16)
            act.dma_start(w1_rows_sb[:, :], w1_rows).then_inc(w1_rows_loaded, 16)
            act.dma_start(w2[:, :, :], W_top2.rearrange("(k p) n -> p k n", p=ROWS)).then_inc(head_loaded, 16)
            act.dma_start(w3[:, :], W_top3.rearrange("(k p) o -> p (k o)", p=ROWS),
                          allow_slow_non_contiguous=True).then_inc(head_loaded, 16)
            act.dma_start(b1[:, :], b_top1.rearrange("(k p) -> p k", p=ROWS),
                          allow_slow_non_contiguous=True).then_inc(head_loaded, 16)
            act.dma_start(b2[:, :], b_top2.rearrange("(k p) -> p k", p=ROWS),
                          allow_slow_non_contiguous=True).then_inc(head_loaded, 16)

            def save_z(b):
                act.wait_ge(prod_used, plan.block_last_half[b] + 1)
                nc.scalar.copy(zT[:, b, :], z_ps[:, :]).then_inc(z_saved, 1)

            saved = 0
            for r in range(plan.rounds):
                for k in fields_to_split(r):
                    act.wait_ge(fields_transposed, k + 1)
                    nc.scalar.copy(x_split[0:DIM, 2 * k, :], t_ps[0:DIM, :])
                    nc.scalar.copy(x_split[DIM:, 2 * k + 1, :], t_ps[DIM:, :])
                    nc.scalar.copy(x_full[:, k, :], t_ps[:, :]).then_inc(x_copied, 1)
                for c in weights_to_split(r):
                    act.wait_ge(raw_loaded[c % RAW_SLOTS], raw_count[c])
                    if c >= SPLIT_SLOTS:
                        act.wait_ge(y_ready, 2 * (c - SPLIT_SLOTS) + 2)
                    nc.scalar.copy(w_hi[:, c % SPLIT_SLOTS, :],
                                   w_raw[:, c % RAW_SLOTS, :, :].rearrange("p n e -> p (n e)")).then_inc(hi_ready, 1)
                while saved < NBLK and plan.block_last_half[saved] < 2 * r:
                    save_z(saved)
                    saved += 1
            while saved < NBLK:
                save_z(saved)
                saved += 1
            act.wait_ge(head_loaded, 64)
            for m in range(M1):
                act.wait_ge(h1_summed, m + 1)
                nc.scalar.activation(h1[:, m, :], h1_ps[m], ACT.Relu, bias=b1[:, m:m + 1]).then_inc(h1_ready, 1)
            for m in range(M2):
                act.wait_ge(h2_summed, m + 1)
                nc.scalar.activation(h2[:, m, :], h2_ps[m], ACT.Relu, bias=b2[:, m:m + 1]).then_inc(h2_ready, 1)
            act.wait_ge(out_summed, 1)
            nc.scalar.copy(y_row, out_ps).then_inc(out_ready, 1)

        @block.vector
        def _(dve):
            def products(h):
                dve.wait_ge(y_ready, h + 1)
                if h >= P_SLOTS:
                    dve.wait_ge(prod_used, h - P_SLOTS + 1)
                for t, n in plan.ops_of_half(h):
                    j = plan.tiles[2 * h + t][1]
                    last = nc.vector.tensor_tensor(
                        prod[:, h % P_SLOTS, t:t + n, :], y_ps[:, h % Y_SLOTS, t:t + n, :],
                        x_full[:, j // 2:j // 2 + n, :], ALU.mult)
                last.then_inc(prod_ready, 1)

            for r in range(plan.rounds):
                for k in fields_to_split(r):
                    dve.wait_ge(x_copied, k + 1)
                    nc.vector.tensor_tensor(x_split[DIM:, 2 * k, :], x_full[0:DIM, k, :],
                                            x_split[0:DIM, 2 * k, :].bitcast(F32), ALU.subtract)
                    nc.vector.tensor_tensor(x_split[0:DIM, 2 * k + 1, :], x_full[DIM:, k, :],
                                            x_split[DIM:, 2 * k + 1, :].bitcast(F32),
                                            ALU.subtract).then_inc(x_ready, 1)
                for c in weights_to_split(r):
                    if not pool_rounds[c]:
                        dve.wait_ge(hi_ready, c + 1)
                        split_lo(nc.vector, c).then_inc(lo_ready_dve, 1)
                products(2 * r)
                products(2 * r + 1)

        @block.tensor
        def _(pe):
            have = {"fields": 0}

            def transpose_fields(k):
                slot = k % GATHER_SLOTS
                pe.wait_ge(fields_gathered[slot], 16 * 2 * BATCH_TILES * (k // GATHER_SLOTS + 1))
                if k:
                    pe.wait_ge(x_copied, k)
                for c in range(BATCH_TILES):
                    last = nc.tensor.transpose(t_ps[:, c * ROWS:(c + 1) * ROWS], gathered[:, slot, c, :], ident[:, :])
                last.then_inc(fields_transposed, 1)

            def interact(h):
                r = h // 2
                if h % 2 == 0:
                    pe.wait_ge(hi_ready, r + 1)
                    wait_lo(pe, r)
                if h >= Y_SLOTS:
                    pe.wait_ge(prod_ready, h - Y_SLOTS + 1)
                for t in range(2):
                    i, j = plan.tiles[2 * h + t]
                    need = max(i, j + 1) // 2 + 1
                    if need > have["fields"]:
                        pe.wait_ge(x_ready, need)
                        have["fields"] = need
                    col = (2 * (h % 2) + t) * ROWS
                    for part, weights in enumerate((w_hi, w_lo)):
                        last = nc.tensor.matmul(y_ps[:, h % Y_SLOTS, t, :], weights[:, r % SPLIT_SLOTS, col:col + ROWS],
                                                x_split[:, i, :], start=(part == 0), stop=(part == 1))
                last.then_inc(y_ready, 1)

            opened = set()
            last_of = {(b, q): max(t for t, at in enumerate(plan.rows) if at[:2] == (b, q))
                       for b, q in {at[:2] for at in plan.rows}}

            def sum_rows(h):
                pe.wait_ge(prod_ready, h + 1)
                for t in range(2):
                    tile = 2 * h + t
                    i, j = plan.tiles[tile]
                    b, q, row = plan.rows[tile]
                    if b and not any((b, s) in opened for s in range(4)):
                        pe.wait_ge(z_saved, b)
                    last = nc.tensor.matmul(
                        z_ps[q * QUAD:(q + 1) * QUAD, :],
                        select[:, int(i == j), QUAD - 1 - row:2 * QUAD - 1 - row],
                        prod[:, h % P_SLOTS, t, :], start=(b, q) not in opened, stop=last_of[b, q] == tile)
                    opened.add((b, q))
                last.then_inc(prod_used, 1)

            pe.wait_ge(tables_loaded, 32)
            pe.wait_ge(dense_loaded, 16)
            for c in range(BATCH_TILES):
                nc.tensor.matmul(z_ps[3 * QUAD:, c * ROWS:(c + 1) * ROWS], dense[:, c, :], ident[:, :],
                                 start=True, stop=True)
            opened.add((0, 3))
            for r in range(plan.rounds):
                for k in fields_to_split(r):
                    transpose_fields(k)
                interact(2 * r)
                interact(2 * r + 1)
                if r:
                    sum_rows(2 * r - 2)
                    sum_rows(2 * r - 1)

            def layer1(m, blocks):
                for b in blocks:
                    last = nc.tensor.matmul(h1_ps[m], w1[:, b, m * ROWS:(m + 1) * ROWS], zT[:, b, :],
                                            start=(b == 0), stop=(b == NBLK - 1))
                return last

            pe.wait_ge(w1_loaded, 16 * NBLK)
            pe.wait_ge(z_saved, NBLK - 1)
            layer1(0, range(NBLK - 1))
            sum_rows(plan.halves - 2)
            sum_rows(plan.halves - 1)
            for m in range(1, M1):
                layer1(m, range(NBLK - 1))
            pe.wait_ge(z_saved, NBLK)
            for m in range(M1):
                layer1(m, [NBLK - 1]).then_inc(h1_summed, 1)
            pe.wait_ge(head_loaded, 64)
            for m in range(M2):
                for k in range(M1):
                    if m == 0:
                        pe.wait_ge(h1_ready, k + 1)
                    last = nc.tensor.matmul(h2_ps[m], w2[:, k, m * ROWS:(m + 1) * ROWS], h1[:, k, :],
                                            start=(k == 0), stop=(k == M1 - 1))
                last.then_inc(h2_summed, 1)
            for k in range(M2):
                pe.wait_ge(h2_ready, k + 1)
                last = nc.tensor.matmul(out_ps, w3[:, k:k + 1], h2[:, k, :], start=(k == 0), stop=(k == M2 - 1))
            last.then_inc(out_summed, 1)


def kernel(**inputs):
    import numpy as np
    import concourse.bacc as bacc
    from concourse.bass_utils import run_bass_kernel_spmd

    plan = Plan()
    identity = np.eye(ROWS, dtype=np.float32)
    selectors = np.zeros((ROWS, 2, 2 * QUAD), np.float32)
    selectors[:DIM, 0, QUAD - 1] = 1.0
    selectors[DIM:, 0, QUAD] = 1.0
    selectors[DIM:, 1, QUAD - 1] = 1.0
    w1_rows = np.array([[b[p] or 0 for b in plan.blocks] for p in range(ROWS)], np.int32)

    nc = bacc.Bacc("TRN2", target_bir_lowering=False, num_devices=1)
    arrays = {}

    def given(name, array):
        array = np.ascontiguousarray(array)
        arrays[name] = array
        return nc.dram_tensor(name, array.shape, mybir.dt.from_np(array.dtype), kind="ExternalInput").ap()

    of = {name: given(f"in_{name}", a) for name, a in inputs.items()}
    tables = [of[f"tbl_{f}"] for f in range(FIELDS)]
    out = nc.dram_tensor("out_0", (BATCH, 1), F32, kind="ExternalOutput").ap()
    dlrm_tower(nc, of["dense_ctx"], of["ids"], tables, of["W_top1"], of["b_top1"], of["W_top2"], of["b_top2"],
               of["W_top3"], of["L0_rec_W"], given("identity", identity), given("selectors", selectors),
               given("w1_rows", w1_rows), out)
    r = run_bass_kernel_spmd(nc, [arrays], core_ids=[0])
    return r.results[0]["out_0"]
```

```python
from contextlib import ExitStack

import concourse.bass as bass
from concourse import mybir

F32 = mybir.dt.float32
F32R = mybir.dt.float32r
I32 = mybir.dt.int32
ALU = mybir.AluOpType
ACT = mybir.ActivationFunctionType

ROWS = 128
BANK = 512
FIELDS = 40
DIM = 64
BATCH = 512
DENSE = 16
BATCH_TILES = BATCH // ROWS
FIELD_PAIRS = FIELDS // 2
PAIRS = FIELDS * (FIELDS - 1) // 2

GROUP_SIZES = [2] * 6 + [4] * 7
HOT_FIELDS = [2, 3]
TABLE_LANES = 125
LANE_ROWS = [8, 10]
HOT_SLOTS = 4
WIDE_IDS_AT = [8, 9, 10, 11, 12, 13, 19]
RAW_TABLES_AT = [14, 16, 18]
SPLIT_TABLES_AT = [24, 28]
HOT_AT = [32, 33, 34, 35]
ROUND = 4
CALM_FROM = 12
CALM = 10
QUAD = 32

GATHER_SLOTS = 7
RAW_SLOTS = 6
SPLIT_SLOTS = 4
Y_SLOTS = 3
P_SLOTS = 6


def pair_index(i, j):
    return i * FIELDS - i * (i + 1) // 2 + (j - i - 1)


class Plan:

    def __init__(self):
        self.tiles = []
        self.group_start = []
        a = 0
        for size in GROUP_SIZES:
            self.group_start.append(len(self.tiles) // ROUND)
            for i in range(a + size - 1):
                first = max(a, i + 1) // 2 * 2
                self.tiles += [(i, j) for j in range(first, a + size, 2)]
            a += size
        assert a == FIELDS
        assert len(self.tiles) % ROUND == 0
        self.rounds = len(self.tiles) // ROUND
        self.halves = 2 * self.rounds
        self.group_start.append(self.rounds)

        self.rows = []
        block, fill, quad = 0, [0, 0, 0, QUAD], 0
        self.blocks = [[None] * ROWS]
        for q in range(DENSE):
            self.blocks[0][3 * QUAD + q] = PAIRS + q
        for t, (i, j) in enumerate(self.tiles):
            n = 1 if i == j else 2
            free = [(quad + s) % 4 for s in range(4) if fill[(quad + s) % 4] + n <= QUAD]
            if t % 2 == 0 and sum((QUAD - f) // 2 for f in fill) < 2:
                block, fill = block + 1, [0] * 4
                self.blocks.append([None] * ROWS)
                free = [quad]
            quad = free[0]
            row = fill[quad]
            self.rows.append((block, quad, row))
            for s in range(n):
                at = j + 1 if n == 1 else j + s
                self.blocks[block][quad * QUAD + row + s] = pair_index(i, at)
            fill[quad] += n
            quad = (quad + 1) % 4
        assert all(fill), "every quadrant of the last block must be written"
        self.block_last_half = [
            max(t for t in range(len(self.tiles)) if self.rows[t][0] == b) // 2 for b in range(len(self.blocks))
        ]

        self.split_round = []
        for g, size in enumerate(GROUP_SIZES):
            before = self.group_start[g] - (self.group_start[g - 1] if g else 0)
            m = size // 2
            for s in range(m):
                lead = 1 + (m - 1 - s) * min(2, before // m)
                self.split_round.append(max(0, self.group_start[g] - lead))

        units = []
        for k, r in enumerate(self.split_round):
            fields = (2 * k, 2 * k + 1)
            units += [(r, 0, (f,)) for f in fields if f in HOT_FIELDS]
            rest = tuple(f for f in fields if f not in HOT_FIELDS)
            units += [(r, 1, rest)] if rest else []
        units.sort(key=lambda unit: unit[:2])
        self.unit_round = [r for r, _, _ in units]
        self.units = [fields for _, _, fields in units]
        self.unit_of = {f: n for n, fields in enumerate(self.units) for f in fields}
        self.hot_fields = [fields[0] for fields in self.units if fields[0] in HOT_FIELDS]

        self.gathered = [n for n, fields in enumerate(self.units) if fields[0] not in HOT_FIELDS]
        self.gathers = []
        for at, n in enumerate(self.gathered):
            free = self.unit_round[self.gathered[at - GATHER_SLOTS]] if at >= GATHER_SLOTS else 0
            for f in self.units[n]:
                k = f // 2
                calm = (k // 2) ** 2 - CALM + 2 * (f % 4) if k >= CALM_FROM else 0
                r = max(free, calm, self.gathers[-1][0] if self.gathers else 0)
                self.gathers.append((min(r, self.unit_round[n]), at, f))

    def hot_before(self, n):
        return len([fields for fields in self.units[:n] if fields[0] in HOT_FIELDS])

    def weight_runs(self, r):
        runs = []
        for s, (i, j) in enumerate(self.tiles[ROUND * r:ROUND * r + ROUND]):
            for e in range(2):
                p = max(0, pair_index(i, j + 1) - 1 + e)
                slot = 2 * s + e
                if runs and runs[-1][0] + runs[-1][1] == p:
                    runs[-1][1] += 1
                else:
                    runs.append([p, 1, slot])
        return runs

    def ops_of_half(self, h):
        (i0, j0), (i1, j1) = self.tiles[2 * h:2 * h + 2]
        return [(0, 2)] if j1 == j0 + 2 else [(0, 1), (1, 1)]

    def splits_on_pool(self, r):
        return r >= 18


def dlrm_tower(nc, dense_ctx, ids, tables, W_top1, b_top1, W_top2, b_top2, W_top3, W, identity, selectors,
               w1_rows, table_rows, out):
    plan = Plan()
    H1 = W_top1.shape[1]
    H2 = W_top2.shape[1]
    M1, M2 = H1 // ROWS, H2 // ROWS
    NBLK = len(plan.blocks)

    with ExitStack() as ctx:
        def sb(name, shape, dt=F32):
            return ctx.enter_context(nc.sbuf_tensor(name, shape, dt))

        def psum(name, shape):
            return ctx.enter_context(nc.psum_tensor(name, shape, F32))

        def sem(name):
            return ctx.enter_context(nc.semaphore(name))

        ids_sb = sb("ids_sb", [ROWS, BATCH_TILES, FIELDS], I32)
        w1_rows_sb = sb("w1_rows_sb", [ROWS, NBLK], I32)
        ident = sb("ident", [ROWS, ROWS])
        select = sb("select", [ROWS, 2, 2 * QUAD])
        ids_float = sb("ids_float", [ROWS, BATCH_TILES, FIELDS])
        table_rows_sb = sb("table_rows_sb", [TABLE_LANES, table_rows.shape[1]])
        dense = sb("dense", [ROWS, BATCH_TILES, QUAD])
        x_full = sb("x_full", [ROWS, FIELD_PAIRS, BATCH])
        x_split = sb("x_split", [ROWS, FIELDS, BATCH], F32R)
        w_raw = sb("w_raw", [ROWS, RAW_SLOTS, 2 * ROUND, DIM])
        w_hi = sb("w_hi", [ROWS, SPLIT_SLOTS, ROUND * ROWS], F32R)
        w_lo = sb("w_lo", [ROWS, SPLIT_SLOTS, ROUND * ROWS], F32R)
        prod = sb("prod", [ROWS, P_SLOTS, 2, BATCH])
        zT = sb("zT", [ROWS, NBLK, BATCH])
        w1 = sb("w1", [ROWS, NBLK, H1])
        gathered = w1[:, :, :].rearrange("p s (c n) -> p s c n", c=BATCH_TILES)
        assert GATHER_SLOTS <= NBLK and H1 == BATCH_TILES * 2 * DIM
        w2 = sb("w2", [ROWS, M1, H2])
        w3 = sb("w3", [ROWS, M2])
        b1 = sb("b1", [ROWS, M1])
        b2 = sb("b2", [ROWS, M2])
        h1 = x_full[:, 0:M1, :]
        h2 = x_full[:, M1:M1 + M2, :]
        y_row = x_full[0:1, M1 + M2, :]

        y_ps = psum("y_ps", [ROWS, Y_SLOTS, 2, BANK])
        z_ps = psum("z_ps", [ROWS, BANK])
        t_ps = psum("t_ps", [ROWS, BANK])
        h1_ps = [t_ps[:, :], y_ps[:, 0, 0, :], y_ps[:, 0, 1, :], y_ps[:, 1, 0, :]]
        h2_ps = [y_ps[:, 1, 1, :], y_ps[:, 2, 0, :]]
        out_ps = y_ps[0:1, 2, 1, :]
        assert M1 == len(h1_ps) and M2 == len(h2_ps)

        ids_loaded = sem("ids_loaded")
        ids_floated = sem("ids_floated")
        ids_spread = sem("ids_spread")
        ids_widened = sem("ids_widened")
        table_loaded = [sem(f"table_loaded{s}") for s in range(len(RAW_TABLES_AT))]
        table_hi_ready = sem("table_hi_ready")
        table_ready = sem("table_ready")
        hot_ready = sem("hot_ready")
        hot_used = sem("hot_used")
        hot_summed = sem("hot_summed")
        hot_copied = sem("hot_copied")
        hot_added = sem("hot_added")
        tables_loaded = sem("tables_loaded")
        head_loaded = sem("head_loaded")
        dense_zeroed = sem("dense_zeroed")
        dense_loaded = sem("dense_loaded")
        w1_rows_loaded = sem("w1_rows_loaded")
        w1_loaded = sem("w1_loaded")
        fields_gathered = [sem(f"fields_gathered{s}") for s in range(GATHER_SLOTS)]
        fields_transposed = sem("fields_transposed")
        x_copied = sem("x_copied")
        x_ready = sem("x_ready")
        raw_loaded = [sem(f"raw_loaded{s}") for s in range(RAW_SLOTS)]
        hi_ready = sem("hi_ready")
        lo_ready_dve = sem("lo_ready_dve")
        lo_ready_pool = sem("lo_ready_pool")
        y_ready = sem("y_ready")
        prod_ready = sem("prod_ready")
        prod_used = sem("prod_used")
        z_saved = sem("z_saved")
        h1_summed = sem("h1_summed")
        h1_ready = sem("h1_ready")
        h2_summed = sem("h2_summed")
        h2_ready = sem("h2_ready")
        out_summed = sem("out_summed")
        out_ready = sem("out_ready")
        out_stored = sem("out_stored")

        raw_count, issued = [], [0] * RAW_SLOTS
        runs = [plan.weight_runs(r) for r in range(plan.rounds)]
        for r in range(plan.rounds):
            issued[r % RAW_SLOTS] += 16 * 2 * len(runs[r])
            raw_count.append(issued[r % RAW_SLOTS])
        pool_rounds = [plan.splits_on_pool(r) for r in range(plan.rounds)]

        def wait_lo(engine, r):
            if pool_rounds[r]:
                engine.wait_ge(lo_ready_pool, sum(pool_rounds[:r + 1]))
            else:
                engine.wait_ge(lo_ready_dve, r + 1 - sum(pool_rounds[:r + 1]))

        def wait_lo_all(engine, r):
            on_pool = sum(pool_rounds[:r + 1])
            if on_pool:
                engine.wait_ge(lo_ready_pool, on_pool)
            if r + 1 - on_pool:
                engine.wait_ge(lo_ready_dve, r + 1 - on_pool)

        lanes = slice(0, TABLE_LANES)
        hot_fields = plan.hot_fields
        per_lane = [tables[f].shape[0] // TABLE_LANES for f in hot_fields]
        assert all(tables[f].shape[0] == TABLE_LANES * n for f, n in zip(hot_fields, per_lane))
        rows_at = {n: sum(LANE_ROWS[:at]) for at, n in enumerate(LANE_ROWS)}
        hot_chunks = [(u, q) for u in range(len(hot_fields)) for q in range(per_lane[u])]

        def wide_ids(u):
            return x_full[lanes, WIDE_IDS_AT[u], :]

        def raw_table(u):
            at = RAW_TABLES_AT[u % len(RAW_TABLES_AT)]
            rows = x_full[lanes, at:at + 2, :].rearrange("p s (q e) -> p (s q) e", e=DIM)
            return rows[:, 0:per_lane[u], :]

        def split_table(u):
            at = SPLIT_TABLES_AT[u % len(SPLIT_TABLES_AT)]
            rows = x_split[lanes, at:at + 4, :].rearrange("p s (q e) -> p (s q) e", e=2 * DIM)
            return rows[:, 0:per_lane[u], :]

        def hot_rows(n):
            return x_split[lanes, HOT_AT[n % HOT_SLOTS], :]

        def spread_bank(u):
            return y_ps[:, u // 2 % Y_SLOTS, u % 2, :]

        def wait_transposes_bank(engine, n):
            if n and plan.units[n - 1][0] in HOT_FIELDS:
                engine.wait_ge(x_ready, n)
            elif n:
                engine.wait_ge(x_copied, n - plan.hot_before(n))

        WEIGHT_LEAD = SPLIT_SLOTS - 1

        def weights_to_split(r):
            if r == 0:
                return range(min(WEIGHT_LEAD + 1, plan.rounds))
            return [r + WEIGHT_LEAD] if r + WEIGHT_LEAD < plan.rounds else []

        def fields_to_split(r):
            return [n for n, at in enumerate(plan.unit_round) if at == r]

        gathered_count, issued = [], [0] * GATHER_SLOTS
        for at, n in enumerate(plan.gathered):
            issued[at % GATHER_SLOTS] += 16 * BATCH_TILES * len(plan.units[n])
            gathered_count.append(issued[at % GATHER_SLOTS])

        def half_of(f):
            return slice(f % 2 * DIM, f % 2 * DIM + DIM)

        def other_half_of(f):
            return slice((1 - f % 2) * DIM, (1 - f % 2) * DIM + DIM)

        def halves_of(fields):
            return slice(fields[0] % 2 * DIM, fields[-1] % 2 * DIM + DIM)

        def split_lo(engine, c):
            slot = c % SPLIT_SLOTS
            return engine.tensor_tensor(
                w_lo[:, slot, :], w_raw[:, c % RAW_SLOTS, :, :].rearrange("p n e -> p (n e)"),
                w_hi[:, slot, :].bitcast(F32), ALU.subtract)

        block = ctx.enter_context(nc.Block())

        @block.sync
        def _(sp):
            sp.dma_start(ids_sb[:, :, :], ids.rearrange("(c p) f -> p c f", p=ROWS)).then_inc(ids_loaded, 16)
            sp.dma_start(table_rows_sb[:, :], table_rows).then_inc(ids_loaded, 16)
            for r in range(plan.rounds):
                slot = r % RAW_SLOTS
                if r >= RAW_SLOTS:
                    wait_lo_all(sp, r - RAW_SLOTS)
                for p, n, at in runs[r]:
                    for half in range(2):
                        sp.dma_start(w_raw[half * DIM:half * DIM + DIM, slot, at:at + n, :],
                                     W[p:p + n, :, :].rearrange("p d e -> d p e")).then_inc(raw_loaded[slot], 16)
            sp.wait_ge(out_ready, 1)
            sp.dma_start(out.rearrange("b o -> o b"), y_row).then_inc(out_stored, 16)
            sp.wait_ge(out_stored, 16)

        @block.gpsimd
        def _(pool):
            def gather(at, field):
                f = field % 2
                slot = at % GATHER_SLOTS
                if at >= GATHER_SLOTS and field == plan.units[plan.gathered[at]][0]:
                    pool.wait_ge(fields_transposed, at - GATHER_SLOTS + 1)
                for c in range(BATCH_TILES):
                    nc.gpsimd.indirect_dma_start(
                        gathered[:, slot, c, f * DIM:f * DIM + DIM], None, tables[field][:, :],
                        bass.IndirectOffsetOnAxis(ap=ids_sb[:, c, field:field + 1], axis=0),
                    ).then_inc(fields_gathered[slot], 16)

            nc.gpsimd.memset(dense[:, :, :], 0.0).then_inc(dense_zeroed, 1)
            pool.wait_ge(ids_loaded, 32)
            for r in range(plan.rounds):
                for when, at, field in plan.gathers:
                    if when == r:
                        gather(at, field)
                for c in weights_to_split(r):
                    if pool_rounds[c]:
                        pool.wait_ge(hi_ready, c + 1)
                        split_lo(nc.gpsimd, c).then_inc(lo_ready_pool, 1)
                if r == plan.unit_round[-1] + 1:
                    pool.wait_ge(w1_rows_loaded, 16)
                    pool.wait_ge(fields_transposed, len(plan.gathered))
                    for b in range(NBLK):
                        nc.gpsimd.indirect_dma_start(
                            w1[:, b, :], None, W_top1[:, :],
                            bass.IndirectOffsetOnAxis(ap=w1_rows_sb[:, b:b + 1], axis=0),
                        ).then_inc(w1_loaded, 16)

        @block.scalar
        def _(act):
            def load_table(u):
                act.dma_start(raw_table(u), tables[hot_fields[u]].rearrange("(p q) e -> p q e", q=per_lane[u])).then_inc(
                    table_loaded[u % len(RAW_TABLES_AT)], 16)

            def hot_unit(n):
                u = plan.hot_before(n)
                act.wait_ge(hot_summed, u + 1)
                nc.scalar.copy(x_split[:, hot_fields[u], :], t_ps[:, :]).then_inc(hot_copied, 1)
                if u + 2 < len(hot_fields):
                    table_hi(u + 2)
                if u + 3 < len(hot_fields):
                    act.wait_ge(table_ready, u + 1)
                    load_table(u + 3)

            def table_hi(u):
                act.wait_ge(table_loaded[u % len(RAW_TABLES_AT)], 16 * (u // len(RAW_TABLES_AT) + 1))
                nc.scalar.copy(split_table(u)[:, :, 0:DIM], raw_table(u)).then_inc(table_hi_ready, 1)

            act.dma_start(ident[:, :], identity).then_inc(tables_loaded, 16)
            for u in range(min(len(hot_fields), len(RAW_TABLES_AT))):
                load_table(u)
            act.dma_start(select[:, :, :], selectors).then_inc(tables_loaded, 16)
            act.wait_ge(dense_zeroed, 1)
            act.dma_start(dense[:, :, 0:DENSE], dense_ctx.rearrange("(c p) q -> p c q", p=ROWS)).then_inc(
                dense_loaded, 16)
            act.dma_start(w1_rows_sb[:, :], w1_rows).then_inc(w1_rows_loaded, 16)
            act.dma_start(w2[:, :, :], W_top2.rearrange("(k p) n -> p k n", p=ROWS)).then_inc(head_loaded, 16)
            act.dma_start(w3[:, :], W_top3.rearrange("(k p) o -> p (k o)", p=ROWS),
                          allow_slow_non_contiguous=True).then_inc(head_loaded, 16)
            act.dma_start(b1[:, :], b_top1.rearrange("(k p) -> p k", p=ROWS),
                          allow_slow_non_contiguous=True).then_inc(head_loaded, 16)
            act.dma_start(b2[:, :], b_top2.rearrange("(k p) -> p k", p=ROWS),
                          allow_slow_non_contiguous=True).then_inc(head_loaded, 16)

            def save_z(b):
                act.wait_ge(prod_used, plan.block_last_half[b] + 1)
                nc.scalar.copy(zT[:, b, :], z_ps[:, :]).then_inc(z_saved, 1)

            for u in range(min(2, len(hot_fields))):
                table_hi(u)
            for u in range(len(hot_fields)):
                act.wait_ge(ids_spread, u + 1)
                nc.scalar.copy(wide_ids(u), spread_bank(u)[lanes, :]).then_inc(ids_widened, 1)
            saved = 0
            for r in range(plan.rounds):
                for n in fields_to_split(r):
                    if plan.units[n][0] in HOT_FIELDS:
                        hot_unit(n)
                        continue
                    act.wait_ge(fields_transposed, n + 1 - plan.hot_before(n))
                    for f in plan.units[n]:
                        own = half_of(f)
                        nc.scalar.copy(x_split[own, f, :], t_ps[own, :])
                    own = halves_of(plan.units[n])
                    nc.scalar.copy(x_full[own, f // 2, :], t_ps[own, :]).then_inc(x_copied, 1)
                for c in weights_to_split(r):
                    act.wait_ge(raw_loaded[c % RAW_SLOTS], raw_count[c])
                    if c >= SPLIT_SLOTS:
                        act.wait_ge(y_ready, 2 * (c - SPLIT_SLOTS) + 2)
                    nc.scalar.copy(w_hi[:, c % SPLIT_SLOTS, :],
                                   w_raw[:, c % RAW_SLOTS, :, :].rearrange("p n e -> p (n e)")).then_inc(hi_ready, 1)
                while saved < NBLK and plan.block_last_half[saved] < 2 * r:
                    save_z(saved)
                    saved += 1
            while saved < NBLK:
                save_z(saved)
                saved += 1
            act.wait_ge(head_loaded, 64)
            for m in range(M1):
                act.wait_ge(h1_summed, m + 1)
                nc.scalar.activation(h1[:, m, :], h1_ps[m], ACT.Relu, bias=b1[:, m:m + 1]).then_inc(h1_ready, 1)
            for m in range(M2):
                act.wait_ge(h2_summed, m + 1)
                nc.scalar.activation(h2[:, m, :], h2_ps[m], ACT.Relu, bias=b2[:, m:m + 1]).then_inc(h2_ready, 1)
            act.wait_ge(out_summed, 1)
            nc.scalar.copy(y_row, out_ps).then_inc(out_ready, 1)

        @block.vector
        def _(dve):
            def products(h):
                dve.wait_ge(y_ready, h + 1)
                if h >= P_SLOTS:
                    dve.wait_ge(prod_used, h - P_SLOTS + 1)
                for t, n in plan.ops_of_half(h):
                    j = plan.tiles[2 * h + t][1]
                    last = nc.vector.tensor_tensor(
                        prod[:, h % P_SLOTS, t:t + n, :], y_ps[:, h % Y_SLOTS, t:t + n, :],
                        x_full[:, j // 2:j // 2 + n, :], ALU.mult)
                last.then_inc(prod_ready, 1)

            def build(u):
                dve.wait_ge(ids_widened, u + 1)
                for q in range(per_lane[u]):
                    n = hot_chunks.index((u, q))
                    if n >= HOT_SLOTS:
                        field, chunk = hot_chunks[n - HOT_SLOTS]
                        if chunk == per_lane[field] - 1:
                            dve.wait_ge(hot_summed, field + 1)
                        else:
                            dve.wait_ge(hot_used, n - HOT_SLOTS - field + 1)
                    row = rows_at[per_lane[u]] + q
                    nc.vector.tensor_scalar(hot_rows(n), wide_ids(u), table_rows_sb[:, row:row + 1], None,
                                            ALU.is_equal).then_inc(hot_ready, 1)

            def table_lo(u):
                dve.wait_ge(table_hi_ready, u + 1)
                nc.vector.tensor_tensor(split_table(u)[:, :, DIM:], raw_table(u),
                                        split_table(u)[:, :, 0:DIM].bitcast(F32), ALU.subtract).then_inc(table_ready, 1)

            def hot_unit(n):
                u = plan.hot_before(n)
                f = hot_fields[u]
                table_lo(u)
                build(u)
                dve.wait_ge(hot_copied, u + 1)
                nc.vector.tensor_tensor(x_full[half_of(f), f // 2, :], t_ps[0:DIM, :],
                                        x_split[DIM:, f, :].bitcast(F32), ALU.add).then_inc(x_ready, 1)

            def split_fields(r):
                for n in fields_to_split(r):
                    if plan.units[n][0] in HOT_FIELDS:
                        hot_unit(n)
                        continue
                    dve.wait_ge(x_copied, n + 1 - plan.hot_before(n))
                    for f in plan.units[n]:
                        last = nc.vector.tensor_tensor(x_split[other_half_of(f), f, :], x_full[half_of(f), f // 2, :],
                                                       x_split[half_of(f), f, :].bitcast(F32), ALU.subtract)
                    last.then_inc(x_ready, 1)

            def split_weights(r):
                for c in weights_to_split(r):
                    if not pool_rounds[c]:
                        dve.wait_ge(hi_ready, c + 1)
                        split_lo(nc.vector, c).then_inc(lo_ready_dve, 1)

            dve.wait_ge(ids_loaded, 32)
            nc.vector.tensor_copy(ids_float[:, :, :], ids_sb[:, :, :]).then_inc(ids_floated, 1)
            for r in range(plan.rounds):
                if r:
                    products(2 * r)
                split_fields(r)
                split_weights(r)
                if not r:
                    products(2 * r)
                products(2 * r + 1)

        @block.tensor
        def _(pe):
            have = {"fields": 0}

            def hot_unit(n):
                u = plan.hot_before(n)
                wait_transposes_bank(pe, n)
                pe.wait_ge(table_ready, u + 1)
                for q in range(per_lane[u]):
                    chunk = hot_chunks.index((u, q))
                    pe.wait_ge(hot_ready, chunk + 1)
                    nc.tensor.matmul(t_ps[:, :], split_table(u)[:, q, :], hot_rows(chunk),
                                     start=(q == 0), stop=(q == per_lane[u] - 1)).then_inc(
                        hot_used if q < per_lane[u] - 1 else hot_summed, 1)

            def transpose_fields(n):
                fields = plan.units[n]
                if fields[0] in HOT_FIELDS:
                    hot_unit(n)
                    return
                at = n - plan.hot_before(n)
                pe.wait_ge(fields_gathered[at % GATHER_SLOTS], gathered_count[at])
                wait_transposes_bank(pe, n)
                own = halves_of(fields)
                for c in range(BATCH_TILES):
                    x = gathered[:, at % GATHER_SLOTS, c, own]
                    if len(fields) == 2:
                        last = nc.tensor.transpose(t_ps[:, c * ROWS:(c + 1) * ROWS], x, ident[:, :])
                    else:
                        last = nc.tensor.matmul(t_ps[own, c * ROWS:(c + 1) * ROWS], x, ident[:, :],
                                                start=True, stop=True)
                last.then_inc(fields_transposed, 1)

            def interact(h):
                r = h // 2
                if h % 2 == 0:
                    pe.wait_ge(hi_ready, r + 1)
                    wait_lo(pe, r)
                if h == 0:
                    pe.wait_ge(ids_widened, len(hot_fields))
                if h >= Y_SLOTS:
                    pe.wait_ge(prod_ready, h - Y_SLOTS + 1)
                for t in range(2):
                    i, j = plan.tiles[2 * h + t]
                    need = max(plan.unit_of[f] for f in (i, j, j + 1)) + 1
                    if need > have["fields"]:
                        pe.wait_ge(x_ready, need)
                        have["fields"] = need
                    col = (2 * (h % 2) + t) * ROWS
                    for part, weights in enumerate((w_hi, w_lo)):
                        last = nc.tensor.matmul(y_ps[:, h % Y_SLOTS, t, :], weights[:, r % SPLIT_SLOTS, col:col + ROWS],
                                                x_split[:, i, :], start=(part == 0), stop=(part == 1))
                last.then_inc(y_ready, 1)

            opened = set()
            last_of = {(b, q): max(t for t, at in enumerate(plan.rows) if at[:2] == (b, q))
                       for b, q in {at[:2] for at in plan.rows}}

            def sum_rows(h):
                pe.wait_ge(prod_ready, h + 1)
                for t in range(2):
                    tile = 2 * h + t
                    i, j = plan.tiles[tile]
                    b, q, row = plan.rows[tile]
                    if b and not any((b, s) in opened for s in range(4)):
                        pe.wait_ge(z_saved, b)
                    last = nc.tensor.matmul(
                        z_ps[q * QUAD:(q + 1) * QUAD, :],
                        select[:, int(i == j), QUAD - 1 - row:2 * QUAD - 1 - row],
                        prod[:, h % P_SLOTS, t, :], start=(b, q) not in opened, stop=last_of[b, q] == tile)
                    opened.add((b, q))
                last.then_inc(prod_used, 1)

            pe.wait_ge(tables_loaded, 32)
            pe.wait_ge(ids_floated, 1)
            for u, field in enumerate(hot_fields):
                if u >= 2 * Y_SLOTS:
                    pe.wait_ge(ids_widened, u - 2 * Y_SLOTS + 1)
                for c in range(BATCH_TILES):
                    last = nc.tensor.matmul(spread_bank(u)[:, c * ROWS:(c + 1) * ROWS],
                                            ids_float[:, c, field:field + 1].broadcast_to([ROWS, ROWS]), ident[:, :],
                                            start=True, stop=True)
                last.then_inc(ids_spread, 1)
            pe.wait_ge(dense_loaded, 16)
            for c in range(BATCH_TILES):
                nc.tensor.matmul(z_ps[3 * QUAD:, c * ROWS:(c + 1) * ROWS], dense[:, c, :], ident[:, :],
                                 start=True, stop=True)
            opened.add((0, 3))
            for r in range(plan.rounds):
                for n in fields_to_split(r):
                    transpose_fields(n)
                interact(2 * r)
                interact(2 * r + 1)
                if r:
                    sum_rows(2 * r - 2)
                    sum_rows(2 * r - 1)

            def layer1(m, blocks):
                for b in blocks:
                    last = nc.tensor.matmul(h1_ps[m], w1[:, b, m * ROWS:(m + 1) * ROWS], zT[:, b, :],
                                            start=(b == 0), stop=(b == NBLK - 1))
                return last

            pe.wait_ge(w1_loaded, 16 * NBLK)
            pe.wait_ge(z_saved, NBLK - 1)
            layer1(0, range(NBLK - 1))
            sum_rows(plan.halves - 2)
            sum_rows(plan.halves - 1)
            for m in range(1, M1):
                layer1(m, range(NBLK - 1))
            pe.wait_ge(z_saved, NBLK)
            for m in range(M1):
                layer1(m, [NBLK - 1]).then_inc(h1_summed, 1)
            pe.wait_ge(head_loaded, 64)
            for m in range(M2):
                for k in range(M1):
                    if m == 0:
                        pe.wait_ge(h1_ready, k + 1)
                    last = nc.tensor.matmul(h2_ps[m], w2[:, k, m * ROWS:(m + 1) * ROWS], h1[:, k, :],
                                            start=(k == 0), stop=(k == M1 - 1))
                last.then_inc(h2_summed, 1)
            for k in range(M2):
                pe.wait_ge(h2_ready, k + 1)
                last = nc.tensor.matmul(out_ps, w3[:, k:k + 1], h2[:, k, :], start=(k == 0), stop=(k == M2 - 1))
            last.then_inc(out_summed, 1)


def kernel(**inputs):
    import numpy as np
    import concourse.bacc as bacc
    from concourse.bass_utils import run_bass_kernel_spmd

    plan = Plan()
    identity = np.eye(ROWS, dtype=np.float32)
    selectors = np.zeros((ROWS, 2, 2 * QUAD), np.float32)
    selectors[:DIM, 0, QUAD - 1] = 1.0
    selectors[DIM:, 0, QUAD] = 1.0
    selectors[DIM:, 1, QUAD - 1] = 1.0
    w1_rows = np.array([[b[p] or 0 for b in plan.blocks] for p in range(ROWS)], np.int32)

    table_rows = np.concatenate(
        [np.arange(TABLE_LANES * n, dtype=np.float32).reshape(TABLE_LANES, n) for n in LANE_ROWS], axis=1)

    nc = bacc.Bacc("TRN2", target_bir_lowering=False, num_devices=1)
    arrays = {}

    def given(name, array):
        array = np.ascontiguousarray(array)
        arrays[name] = array
        return nc.dram_tensor(name, array.shape, mybir.dt.from_np(array.dtype), kind="ExternalInput").ap()

    of = {name: given(f"in_{name}", a) for name, a in inputs.items()}
    tables = [of[f"tbl_{f}"] for f in range(FIELDS)]
    out = nc.dram_tensor("out_0", (BATCH, 1), F32, kind="ExternalOutput").ap()
    dlrm_tower(nc, of["dense_ctx"], of["ids"], tables, of["W_top1"], of["b_top1"], of["W_top2"], of["b_top2"],
               of["W_top3"], of["L0_rec_W"], given("identity", identity), given("selectors", selectors),
               given("w1_rows", w1_rows), given("table_rows", table_rows), out)
    r = run_bass_kernel_spmd(nc, [arrays], core_ids=[0])
    return r.results[0]["out_0"]
```

```python
from contextlib import ExitStack

import concourse.bass as bass
from concourse import mybir

F32 = mybir.dt.float32
F32R = mybir.dt.float32r
I32 = mybir.dt.int32
ALU = mybir.AluOpType
ACT = mybir.ActivationFunctionType

ROWS = 128
BANK = 512
FIELDS = 40
DIM = 64
BATCH = 512
DENSE = 16
BATCH_TILES = BATCH // ROWS
FIELD_PAIRS = FIELDS // 2
PAIRS = FIELDS * (FIELDS - 1) // 2

GROUP_SIZES = [2] * 6 + [4] * 7
HOT_FIELDS = [2, 3]
TABLE_LANES = 125
HOT_SLOTS = 4
WIDE_IDS_AT = [8, 9]
RAW_TABLES_AT = [14, 15]
SPLIT_TABLES_AT = [24, 26]
HOT_AT = [32, 33, 34, 35]
ROUND = 4
CALM_FROM = 11
CALM = 12
QUAD = 32

GATHER_SLOTS = 7
RAW_SLOTS = 6
SPLIT_SLOTS = 4
Y_SLOTS = 3
P_SLOTS = 6


def pair_index(i, j):
    return i * FIELDS - i * (i + 1) // 2 + (j - i - 1)


class Plan:

    def __init__(self):
        self.tiles = []
        self.group_start = []
        a = 0
        for size in GROUP_SIZES:
            self.group_start.append(len(self.tiles) // ROUND)
            for i in range(a + size - 1):
                first = max(a, i + 1) // 2 * 2
                self.tiles += [(i, j) for j in range(first, a + size, 2)]
            a += size
        assert a == FIELDS
        assert len(self.tiles) % ROUND == 0
        self.rounds = len(self.tiles) // ROUND
        self.halves = 2 * self.rounds
        self.group_start.append(self.rounds)

        self.rows = []
        block, fill, quad = 0, [0, 0, 0, QUAD], 0
        self.blocks = [[None] * ROWS]
        for q in range(DENSE):
            self.blocks[0][3 * QUAD + q] = PAIRS + q
        for t, (i, j) in enumerate(self.tiles):
            n = 1 if i == j else 2
            free = [(quad + s) % 4 for s in range(4) if fill[(quad + s) % 4] + n <= QUAD]
            if t % 2 == 0 and sum((QUAD - f) // 2 for f in fill) < 2:
                block, fill = block + 1, [0] * 4
                self.blocks.append([None] * ROWS)
                free = [quad]
            quad = free[0]
            row = fill[quad]
            self.rows.append((block, quad, row))
            for s in range(n):
                at = j + 1 if n == 1 else j + s
                self.blocks[block][quad * QUAD + row + s] = pair_index(i, at)
            fill[quad] += n
            quad = (quad + 1) % 4
        assert all(fill), "every quadrant of the last block must be written"
        self.block_last_half = [
            max(t for t in range(len(self.tiles)) if self.rows[t][0] == b) // 2 for b in range(len(self.blocks))
        ]

        self.split_round = []
        for g, size in enumerate(GROUP_SIZES):
            before = self.group_start[g] - (self.group_start[g - 1] if g else 0)
            m = size // 2
            for s in range(m):
                lead = 1 + (m - 1 - s) * min(2, before // m)
                self.split_round.append(max(0, self.group_start[g] - lead))

        units = []
        for k, r in enumerate(self.split_round):
            if 2 * k in HOT_FIELDS:
                assert r == 0 and 2 * k + 1 in HOT_FIELDS
                units += [(r, 0, (2 * k,)), (r, 0, (2 * k + 1,))]
            else:
                units.append((r, 1, (2 * k, 2 * k + 1)))
        units.sort(key=lambda unit: unit[:2])
        self.unit_round = [r for r, _, _ in units]
        self.units = [fields for _, _, fields in units]
        self.unit_of = {f: n for n, fields in enumerate(self.units) for f in fields}
        self.hot_fields = [fields[0] for fields in self.units if len(fields) == 1]

        self.gathered = [n for n, fields in enumerate(self.units) if fields[0] not in HOT_FIELDS]
        self.gathers = []
        for at, n in enumerate(self.gathered):
            free = self.unit_round[self.gathered[at - GATHER_SLOTS]] if at >= GATHER_SLOTS else 0
            for f in self.units[n]:
                k = f // 2
                calm = (k // 2) ** 2 - CALM + 2 * (f % 4) if k >= CALM_FROM else 0
                r = max(free, calm, self.gathers[-1][0] if self.gathers else 0)
                self.gathers.append((min(r, self.unit_round[n]), at, f))

    def hot_before(self, n):
        return len([fields for fields in self.units[:n] if fields[0] in HOT_FIELDS])

    def weight_runs(self, r):
        runs = []
        for s, (i, j) in enumerate(self.tiles[ROUND * r:ROUND * r + ROUND]):
            for e in range(2):
                p = max(0, pair_index(i, j + 1) - 1 + e)
                slot = 2 * s + e
                if runs and runs[-1][0] + runs[-1][1] == p:
                    runs[-1][1] += 1
                else:
                    runs.append([p, 1, slot])
        return runs

    def ops_of_half(self, h):
        (i0, j0), (i1, j1) = self.tiles[2 * h:2 * h + 2]
        return [(0, 2)] if j1 == j0 + 2 else [(0, 1), (1, 1)]

    def splits_on_pool(self, r):
        return r >= 18


def dlrm_tower(nc, dense_ctx, ids, tables, W_top1, b_top1, W_top2, b_top2, W_top3, W, identity, selectors,
               w1_rows, table_rows, out):
    plan = Plan()
    H1 = W_top1.shape[1]
    H2 = W_top2.shape[1]
    M1, M2 = H1 // ROWS, H2 // ROWS
    NBLK = len(plan.blocks)

    with ExitStack() as ctx:
        def sb(name, shape, dt=F32):
            return ctx.enter_context(nc.sbuf_tensor(name, shape, dt))

        def psum(name, shape):
            return ctx.enter_context(nc.psum_tensor(name, shape, F32))

        def sem(name):
            return ctx.enter_context(nc.semaphore(name))

        ids_sb = sb("ids_sb", [ROWS, BATCH_TILES, FIELDS], I32)
        w1_rows_sb = sb("w1_rows_sb", [ROWS, NBLK], I32)
        ident = sb("ident", [ROWS, ROWS])
        select = sb("select", [ROWS, 2, 2 * QUAD])
        ids_float = sb("ids_float", [ROWS, BATCH_TILES, FIELDS])
        table_rows_sb = sb("table_rows_sb", [TABLE_LANES, table_rows.shape[1]])
        dense = sb("dense", [ROWS, BATCH_TILES, QUAD])
        x_full = sb("x_full", [ROWS, FIELD_PAIRS, BATCH])
        x_split = sb("x_split", [ROWS, FIELDS, BATCH], F32R)
        w_raw = sb("w_raw", [ROWS, RAW_SLOTS, 2 * ROUND, DIM])
        w_hi = sb("w_hi", [ROWS, SPLIT_SLOTS, ROUND * ROWS], F32R)
        w_lo = sb("w_lo", [ROWS, SPLIT_SLOTS, ROUND * ROWS], F32R)
        prod = sb("prod", [ROWS, P_SLOTS, 2, BATCH])
        zT = sb("zT", [ROWS, NBLK, BATCH])
        w1 = sb("w1", [ROWS, NBLK, H1])
        gathered = w1[:, :, :].rearrange("p s (c n) -> p s c n", c=BATCH_TILES)
        assert GATHER_SLOTS <= NBLK and H1 == BATCH_TILES * 2 * DIM
        w2 = sb("w2", [ROWS, M1, H2])
        w3 = sb("w3", [ROWS, M2])
        b1 = sb("b1", [ROWS, M1])
        b2 = sb("b2", [ROWS, M2])
        h1 = x_full[:, 0:M1, :]
        h2 = x_full[:, M1:M1 + M2, :]
        y_row = x_full[0:1, M1 + M2, :]

        y_ps = psum("y_ps", [ROWS, Y_SLOTS, 2, BANK])
        z_ps = psum("z_ps", [ROWS, BANK])
        t_ps = psum("t_ps", [ROWS, BANK])
        h1_ps = [t_ps[:, :], y_ps[:, 0, 0, :], y_ps[:, 0, 1, :], y_ps[:, 1, 0, :]]
        h2_ps = [y_ps[:, 1, 1, :], y_ps[:, 2, 0, :]]
        out_ps = y_ps[0:1, 2, 1, :]
        assert M1 == len(h1_ps) and M2 == len(h2_ps)

        ids_loaded = sem("ids_loaded")
        ids_floated = sem("ids_floated")
        ids_spread = sem("ids_spread")
        ids_widened = sem("ids_widened")
        table_loaded = [sem(f"table_loaded{u}") for u in range(len(RAW_TABLES_AT))]
        table_rows_loaded = sem("table_rows_loaded")
        table_hi_ready = sem("table_hi_ready")
        table_ready = sem("table_ready")
        hot_ready = sem("hot_ready")
        hot_used = sem("hot_used")
        hot_copied = sem("hot_copied")
        tables_loaded = sem("tables_loaded")
        head_loaded = sem("head_loaded")
        dense_zeroed = sem("dense_zeroed")
        dense_loaded = sem("dense_loaded")
        w1_rows_loaded = sem("w1_rows_loaded")
        w1_loaded = sem("w1_loaded")
        fields_gathered = [sem(f"fields_gathered{s}") for s in range(GATHER_SLOTS)]
        fields_transposed = sem("fields_transposed")
        x_copied = sem("x_copied")
        x_ready = sem("x_ready")
        raw_loaded = [sem(f"raw_loaded{s}") for s in range(RAW_SLOTS)]
        hi_ready = sem("hi_ready")
        lo_ready_dve = sem("lo_ready_dve")
        lo_ready_pool = sem("lo_ready_pool")
        y_ready = sem("y_ready")
        prod_ready = sem("prod_ready")
        prod_used = sem("prod_used")
        z_saved = sem("z_saved")
        h1_summed = sem("h1_summed")
        h1_ready = sem("h1_ready")
        h2_summed = sem("h2_summed")
        h2_ready = sem("h2_ready")
        out_summed = sem("out_summed")
        out_ready = sem("out_ready")
        out_stored = sem("out_stored")

        raw_count, issued = [], [0] * RAW_SLOTS
        runs = [plan.weight_runs(r) for r in range(plan.rounds)]
        for r in range(plan.rounds):
            issued[r % RAW_SLOTS] += 16 * 2 * len(runs[r])
            raw_count.append(issued[r % RAW_SLOTS])
        pool_rounds = [plan.splits_on_pool(r) for r in range(plan.rounds)]

        def wait_lo(engine, r):
            if pool_rounds[r]:
                engine.wait_ge(lo_ready_pool, sum(pool_rounds[:r + 1]))
            else:
                engine.wait_ge(lo_ready_dve, r + 1 - sum(pool_rounds[:r + 1]))

        def wait_lo_all(engine, r):
            on_pool = sum(pool_rounds[:r + 1])
            if on_pool:
                engine.wait_ge(lo_ready_pool, on_pool)
            if r + 1 - on_pool:
                engine.wait_ge(lo_ready_dve, r + 1 - on_pool)

        lanes = slice(0, TABLE_LANES)
        hot_fields = plan.hot_fields
        per_lane = table_rows.shape[1]
        assert all(tables[f].shape[0] == TABLE_LANES * per_lane for f in hot_fields)
        assert len(hot_fields) == len(WIDE_IDS_AT) == len(RAW_TABLES_AT) == len(SPLIT_TABLES_AT) <= 2 * Y_SLOTS

        def wide_ids(u):
            return x_full[lanes, WIDE_IDS_AT[u], :]

        def raw_table(u):
            return x_full[lanes, RAW_TABLES_AT[u], :].rearrange("p (q e) -> p q e", e=DIM)

        def split_table(u):
            at = SPLIT_TABLES_AT[u]
            return x_split[lanes, at:at + 2, :].rearrange("p s (q e) -> p (s q) e", e=2 * DIM)

        def hot_rows(n):
            return x_split[lanes, HOT_AT[n % HOT_SLOTS], :]

        def spread_bank(u):
            return y_ps[:, u // 2, u % 2, :]

        def wait_transposes_bank(engine, n):
            if n and plan.units[n - 1][0] in HOT_FIELDS:
                engine.wait_ge(x_ready, n)
            elif n:
                engine.wait_ge(x_copied, n - plan.hot_before(n))

        WEIGHT_LEAD = SPLIT_SLOTS - 1

        def weights_to_split(r):
            if r == 0:
                return range(min(WEIGHT_LEAD + 1, plan.rounds))
            return [r + WEIGHT_LEAD] if r + WEIGHT_LEAD < plan.rounds else []

        def fields_to_split(r):
            return [n for n, at in enumerate(plan.unit_round) if at == r]

        def half_of(f):
            return slice(f % 2 * DIM, f % 2 * DIM + DIM)

        def other_half_of(f):
            return slice((1 - f % 2) * DIM, (1 - f % 2) * DIM + DIM)

        def split_lo(engine, c):
            slot = c % SPLIT_SLOTS
            return engine.tensor_tensor(
                w_lo[:, slot, :], w_raw[:, c % RAW_SLOTS, :, :].rearrange("p n e -> p (n e)"),
                w_hi[:, slot, :].bitcast(F32), ALU.subtract)

        block = ctx.enter_context(nc.Block())

        @block.sync
        def _(sp):
            sp.dma_start(ids_sb[:, :, :], ids.rearrange("(c p) f -> p c f", p=ROWS)).then_inc(ids_loaded, 16)
            sp.dma_start(table_rows_sb[:, :], table_rows).then_inc(table_rows_loaded, 16)
            for r in range(plan.rounds):
                slot = r % RAW_SLOTS
                if r >= RAW_SLOTS:
                    wait_lo_all(sp, r - RAW_SLOTS)
                for p, n, at in runs[r]:
                    for half in range(2):
                        sp.dma_start(w_raw[half * DIM:half * DIM + DIM, slot, at:at + n, :],
                                     W[p:p + n, :, :].rearrange("p d e -> d p e")).then_inc(raw_loaded[slot], 16)
            sp.wait_ge(out_ready, 1)
            sp.dma_start(out.rearrange("b o -> o b"), y_row).then_inc(out_stored, 16)
            sp.wait_ge(out_stored, 16)

        @block.gpsimd
        def _(pool):
            def gather(at, field):
                f = field % 2
                slot = at % GATHER_SLOTS
                if at >= GATHER_SLOTS and field == plan.units[plan.gathered[at]][0]:
                    pool.wait_ge(fields_transposed, at - GATHER_SLOTS + 1)
                for c in range(BATCH_TILES):
                    nc.gpsimd.indirect_dma_start(
                        gathered[:, slot, c, f * DIM:f * DIM + DIM], None, tables[field][:, :],
                        bass.IndirectOffsetOnAxis(ap=ids_sb[:, c, field:field + 1], axis=0),
                    ).then_inc(fields_gathered[slot], 16)

            nc.gpsimd.memset(dense[:, :, :], 0.0).then_inc(dense_zeroed, 1)
            pool.wait_ge(ids_loaded, 16)
            for r in range(plan.rounds):
                for when, at, field in plan.gathers:
                    if when == r:
                        gather(at, field)
                for c in weights_to_split(r):
                    if pool_rounds[c]:
                        pool.wait_ge(hi_ready, c + 1)
                        split_lo(nc.gpsimd, c).then_inc(lo_ready_pool, 1)
                if r == plan.unit_round[-1] + 1:
                    pool.wait_ge(w1_rows_loaded, 16)
                    pool.wait_ge(fields_transposed, len(plan.gathered))
                    for b in range(NBLK):
                        nc.gpsimd.indirect_dma_start(
                            w1[:, b, :], None, W_top1[:, :],
                            bass.IndirectOffsetOnAxis(ap=w1_rows_sb[:, b:b + 1], axis=0),
                        ).then_inc(w1_loaded, 16)

        @block.scalar
        def _(act):
            def load_table(u):
                act.dma_start(raw_table(u), tables[hot_fields[u]].rearrange("(p q) e -> p q e", q=per_lane)).then_inc(
                    table_loaded[u], 16)

            def hot_unit(n):
                u = plan.hot_before(n)
                act.wait_ge(hot_used, per_lane * (u + 1))
                nc.scalar.copy(x_split[:, hot_fields[u], :], t_ps[:, :]).then_inc(hot_copied, 1)

            def table_hi(u):
                act.wait_ge(table_loaded[u], 16)
                nc.scalar.copy(split_table(u)[:, :, 0:DIM], raw_table(u)).then_inc(table_hi_ready, 1)

            act.dma_start(ident[:, :], identity).then_inc(tables_loaded, 16)
            for u in range(len(hot_fields)):
                load_table(u)
            act.dma_start(select[:, :, :], selectors).then_inc(tables_loaded, 16)
            act.wait_ge(dense_zeroed, 1)
            act.dma_start(dense[:, :, 0:DENSE], dense_ctx.rearrange("(c p) q -> p c q", p=ROWS)).then_inc(
                dense_loaded, 16)
            act.dma_start(w1_rows_sb[:, :], w1_rows).then_inc(w1_rows_loaded, 16)
            act.dma_start(w2[:, :, :], W_top2.rearrange("(k p) n -> p k n", p=ROWS)).then_inc(head_loaded, 16)
            act.dma_start(w3[:, :], W_top3.rearrange("(k p) o -> p (k o)", p=ROWS),
                          allow_slow_non_contiguous=True).then_inc(head_loaded, 16)
            act.dma_start(b1[:, :], b_top1.rearrange("(k p) -> p k", p=ROWS),
                          allow_slow_non_contiguous=True).then_inc(head_loaded, 16)
            act.dma_start(b2[:, :], b_top2.rearrange("(k p) -> p k", p=ROWS),
                          allow_slow_non_contiguous=True).then_inc(head_loaded, 16)

            def save_z(b):
                act.wait_ge(prod_used, plan.block_last_half[b] + 1)
                nc.scalar.copy(zT[:, b, :], z_ps[:, :]).then_inc(z_saved, 1)

            for u in range(len(hot_fields)):
                table_hi(u)
            for u in range(len(hot_fields)):
                act.wait_ge(ids_spread, u + 1)
                nc.scalar.copy(wide_ids(u), spread_bank(u)[lanes, :]).then_inc(ids_widened, 1)
            saved = 0
            for r in range(plan.rounds):
                for n in fields_to_split(r):
                    if plan.units[n][0] in HOT_FIELDS:
                        hot_unit(n)
                        continue
                    act.wait_ge(fields_transposed, n + 1 - plan.hot_before(n))
                    for f in plan.units[n]:
                        own = half_of(f)
                        nc.scalar.copy(x_split[own, f, :], t_ps[own, :])
                    nc.scalar.copy(x_full[:, f // 2, :], t_ps[:, :]).then_inc(x_copied, 1)
                for c in weights_to_split(r):
                    act.wait_ge(raw_loaded[c % RAW_SLOTS], raw_count[c])
                    if c >= SPLIT_SLOTS:
                        act.wait_ge(y_ready, 2 * (c - SPLIT_SLOTS) + 2)
                    nc.scalar.copy(w_hi[:, c % SPLIT_SLOTS, :],
                                   w_raw[:, c % RAW_SLOTS, :, :].rearrange("p n e -> p (n e)")).then_inc(hi_ready, 1)
                while saved < NBLK and plan.block_last_half[saved] < 2 * r:
                    save_z(saved)
                    saved += 1
            while saved < NBLK:
                save_z(saved)
                saved += 1
            act.wait_ge(head_loaded, 64)
            for m in range(M1):
                act.wait_ge(h1_summed, m + 1)
                nc.scalar.activation(h1[:, m, :], h1_ps[m], ACT.Relu, bias=b1[:, m:m + 1]).then_inc(h1_ready, 1)
            for m in range(M2):
                act.wait_ge(h2_summed, m + 1)
                nc.scalar.activation(h2[:, m, :], h2_ps[m], ACT.Relu, bias=b2[:, m:m + 1]).then_inc(h2_ready, 1)
            act.wait_ge(out_summed, 1)
            nc.scalar.copy(y_row, out_ps).then_inc(out_ready, 1)

        @block.vector
        def _(dve):
            def products(h):
                dve.wait_ge(y_ready, h + 1)
                if h >= P_SLOTS:
                    dve.wait_ge(prod_used, h - P_SLOTS + 1)
                for t, n in plan.ops_of_half(h):
                    j = plan.tiles[2 * h + t][1]
                    last = nc.vector.tensor_tensor(
                        prod[:, h % P_SLOTS, t:t + n, :], y_ps[:, h % Y_SLOTS, t:t + n, :],
                        x_full[:, j // 2:j // 2 + n, :], ALU.mult)
                last.then_inc(prod_ready, 1)

            def build(u):
                dve.wait_ge(ids_widened, u + 1)
                for q in range(per_lane):
                    n = per_lane * u + q
                    if n >= HOT_SLOTS:
                        dve.wait_ge(hot_used, n - HOT_SLOTS + 1)
                    nc.vector.tensor_scalar(hot_rows(n), wide_ids(u), table_rows_sb[:, q:q + 1], None,
                                            ALU.is_equal).then_inc(hot_ready, 1)

            def table_lo(u):
                dve.wait_ge(table_hi_ready, u + 1)
                nc.vector.tensor_tensor(split_table(u)[:, :, DIM:], raw_table(u),
                                        split_table(u)[:, :, 0:DIM].bitcast(F32), ALU.subtract).then_inc(table_ready, 1)

            def hot_unit(n):
                u = plan.hot_before(n)
                f = hot_fields[u]
                table_lo(u)
                build(u)
                dve.wait_ge(hot_copied, u + 1)
                nc.vector.tensor_tensor(x_full[half_of(f), f // 2, :], t_ps[0:DIM, :],
                                        x_split[DIM:, f, :].bitcast(F32), ALU.add).then_inc(x_ready, 1)

            def split_fields(r):
                for n in fields_to_split(r):
                    if plan.units[n][0] in HOT_FIELDS:
                        hot_unit(n)
                        continue
                    dve.wait_ge(x_copied, n + 1 - plan.hot_before(n))
                    for f in plan.units[n]:
                        last = nc.vector.tensor_tensor(x_split[other_half_of(f), f, :], x_full[half_of(f), f // 2, :],
                                                       x_split[half_of(f), f, :].bitcast(F32), ALU.subtract)
                    last.then_inc(x_ready, 1)

            def split_weights(r):
                for c in weights_to_split(r):
                    if not pool_rounds[c]:
                        dve.wait_ge(hi_ready, c + 1)
                        split_lo(nc.vector, c).then_inc(lo_ready_dve, 1)

            dve.wait_ge(ids_loaded, 16)
            nc.vector.tensor_copy(ids_float[:, :, :], ids_sb[:, :, :]).then_inc(ids_floated, 1)
            dve.wait_ge(table_rows_loaded, 16)
            for r in range(plan.rounds):
                if r:
                    products(2 * r)
                split_fields(r)
                split_weights(r)
                if not r:
                    products(2 * r)
                products(2 * r + 1)

        @block.tensor
        def _(pe):
            have = {"fields": 0}

            def hot_unit(n):
                u = plan.hot_before(n)
                wait_transposes_bank(pe, n)
                pe.wait_ge(table_ready, u + 1)
                for q in range(per_lane):
                    pe.wait_ge(hot_ready, per_lane * u + q + 1)
                    nc.tensor.matmul(t_ps[:, :], split_table(u)[:, q, :], hot_rows(per_lane * u + q),
                                     start=(q == 0), stop=(q == per_lane - 1)).then_inc(hot_used, 1)

            def transpose_fields(n):
                if plan.units[n][0] in HOT_FIELDS:
                    hot_unit(n)
                    return
                at = n - plan.hot_before(n)
                pe.wait_ge(fields_gathered[at % GATHER_SLOTS], 16 * 2 * BATCH_TILES * (at // GATHER_SLOTS + 1))
                wait_transposes_bank(pe, n)
                for c in range(BATCH_TILES):
                    last = nc.tensor.transpose(t_ps[:, c * ROWS:(c + 1) * ROWS],
                                               gathered[:, at % GATHER_SLOTS, c, :], ident[:, :])
                last.then_inc(fields_transposed, 1)

            def interact(h):
                r = h // 2
                if h % 2 == 0:
                    pe.wait_ge(hi_ready, r + 1)
                    wait_lo(pe, r)
                if h == 0:
                    pe.wait_ge(ids_widened, len(hot_fields))
                if h >= Y_SLOTS:
                    pe.wait_ge(prod_ready, h - Y_SLOTS + 1)
                for t in range(2):
                    i, j = plan.tiles[2 * h + t]
                    need = max(plan.unit_of[f] for f in (i, j, j + 1)) + 1
                    if need > have["fields"]:
                        pe.wait_ge(x_ready, need)
                        have["fields"] = need
                    col = (2 * (h % 2) + t) * ROWS
                    for part, weights in enumerate((w_hi, w_lo)):
                        last = nc.tensor.matmul(y_ps[:, h % Y_SLOTS, t, :], weights[:, r % SPLIT_SLOTS, col:col + ROWS],
                                                x_split[:, i, :], start=(part == 0), stop=(part == 1))
                last.then_inc(y_ready, 1)

            opened = set()
            last_of = {(b, q): max(t for t, at in enumerate(plan.rows) if at[:2] == (b, q))
                       for b, q in {at[:2] for at in plan.rows}}

            def sum_rows(h):
                pe.wait_ge(prod_ready, h + 1)
                for t in range(2):
                    tile = 2 * h + t
                    i, j = plan.tiles[tile]
                    b, q, row = plan.rows[tile]
                    if b and not any((b, s) in opened for s in range(4)):
                        pe.wait_ge(z_saved, b)
                    last = nc.tensor.matmul(
                        z_ps[q * QUAD:(q + 1) * QUAD, :],
                        select[:, int(i == j), QUAD - 1 - row:2 * QUAD - 1 - row],
                        prod[:, h % P_SLOTS, t, :], start=(b, q) not in opened, stop=last_of[b, q] == tile)
                    opened.add((b, q))
                last.then_inc(prod_used, 1)

            pe.wait_ge(tables_loaded, 32)
            pe.wait_ge(ids_floated, 1)
            for u, field in enumerate(hot_fields):
                for c in range(BATCH_TILES):
                    last = nc.tensor.matmul(spread_bank(u)[:, c * ROWS:(c + 1) * ROWS],
                                            ids_float[:, c, field:field + 1].broadcast_to([ROWS, ROWS]), ident[:, :],
                                            start=True, stop=True)
                last.then_inc(ids_spread, 1)
            pe.wait_ge(dense_loaded, 16)
            for c in range(BATCH_TILES):
                nc.tensor.matmul(z_ps[3 * QUAD:, c * ROWS:(c + 1) * ROWS], dense[:, c, :], ident[:, :],
                                 start=True, stop=True)
            opened.add((0, 3))
            for r in range(plan.rounds):
                for n in fields_to_split(r):
                    transpose_fields(n)
                interact(2 * r)
                interact(2 * r + 1)
                if r:
                    sum_rows(2 * r - 2)
                    sum_rows(2 * r - 1)

            def layer1(m, blocks):
                for b in blocks:
                    last = nc.tensor.matmul(h1_ps[m], w1[:, b, m * ROWS:(m + 1) * ROWS], zT[:, b, :],
                                            start=(b == 0), stop=(b == NBLK - 1))
                return last

            pe.wait_ge(w1_loaded, 16 * NBLK)
            pe.wait_ge(z_saved, NBLK - 1)
            layer1(0, range(NBLK - 1))
            sum_rows(plan.halves - 2)
            sum_rows(plan.halves - 1)
            for m in range(1, M1):
                layer1(m, range(NBLK - 1))
            pe.wait_ge(z_saved, NBLK)
            for m in range(M1):
                layer1(m, [NBLK - 1]).then_inc(h1_summed, 1)
            pe.wait_ge(head_loaded, 64)
            for m in range(M2):
                for k in range(M1):
                    if m == 0:
                        pe.wait_ge(h1_ready, k + 1)
                    last = nc.tensor.matmul(h2_ps[m], w2[:, k, m * ROWS:(m + 1) * ROWS], h1[:, k, :],
                                            start=(k == 0), stop=(k == M1 - 1))
                last.then_inc(h2_summed, 1)
            for k in range(M2):
                pe.wait_ge(h2_ready, k + 1)
                last = nc.tensor.matmul(out_ps, w3[:, k:k + 1], h2[:, k, :], start=(k == 0), stop=(k == M2 - 1))
            last.then_inc(out_summed, 1)


def kernel(**inputs):
    import numpy as np
    import concourse.bacc as bacc
    from concourse.bass_utils import run_bass_kernel_spmd

    plan = Plan()
    identity = np.eye(ROWS, dtype=np.float32)
    selectors = np.zeros((ROWS, 2, 2 * QUAD), np.float32)
    selectors[:DIM, 0, QUAD - 1] = 1.0
    selectors[DIM:, 0, QUAD] = 1.0
    selectors[DIM:, 1, QUAD - 1] = 1.0
    w1_rows = np.array([[b[p] or 0 for b in plan.blocks] for p in range(ROWS)], np.int32)

    hot_rows = inputs[f"tbl_{HOT_FIELDS[0]}"].shape[0]
    table_rows = np.arange(hot_rows, dtype=np.float32).reshape(TABLE_LANES, -1)

    nc = bacc.Bacc("TRN2", target_bir_lowering=False, num_devices=1)
    arrays = {}

    def given(name, array):
        array = np.ascontiguousarray(array)
        arrays[name] = array
        return nc.dram_tensor(name, array.shape, mybir.dt.from_np(array.dtype), kind="ExternalInput").ap()

    of = {name: given(f"in_{name}", a) for name, a in inputs.items()}
    tables = [of[f"tbl_{f}"] for f in range(FIELDS)]
    out = nc.dram_tensor("out_0", (BATCH, 1), F32, kind="ExternalOutput").ap()
    dlrm_tower(nc, of["dense_ctx"], of["ids"], tables, of["W_top1"], of["b_top1"], of["W_top2"], of["b_top2"],
               of["W_top3"], of["L0_rec_W"], given("identity", identity), given("selectors", selectors),
               given("w1_rows", w1_rows), given("table_rows", table_rows), out)
    r = run_bass_kernel_spmd(nc, [arrays], core_ids=[0])
    return r.results[0]["out_0"]
```
